# Optimizing a Trainium2 kernel written in Bass

```python
import numpy as np
import jax
import jax.numpy as jnp

def _softmax(x, axis=-1):
    return jax.nn.softmax(x, axis=axis)

def _gelu(x):
    return jax.nn.gelu(x, approximate=True)

def _silu(x):
    return jax.nn.silu(x)

def _sigmoid(x):
    return jax.nn.sigmoid(x)

def _layernorm(x, axis=-1, eps=1e-05):
    m = jnp.mean(x, axis=axis, keepdims=True)
    v = jnp.var(x, axis=axis, keepdims=True)
    return (x - m) / jnp.sqrt(v + eps)

def _scatter_add(tgt, idx, src, axis=0):
    return tgt.at[idx].add(src)

def _segment_sum(src, seg, n):
    return jax.ops.segment_sum(src, seg, n)
kernel_name = 'mk_gnn_preln_d1_gnn_r8_06bf6d'

def setup_inputs(seed: int=0):
    np.random.seed(seed)
    _w = jnp.asarray

    def _rec_inputs():
        import jax
        import jax.numpy as jnp
        _gk = jax.random.key(seed)
        x = -0.0003713 + 1 * jax.random.normal(jax.random.fold_in(_gk, 1), (12500, 256), jnp.float32)
        _s = jax.random.randint(jax.random.fold_in(_gk, 2), (100000,), 0, 12500, jnp.int32)
        _d = jax.random.randint(jax.random.fold_in(_gk, 3), (100000,), 0, 12500, jnp.int32)
        _loop = jnp.arange(12500, dtype=jnp.int32)
        src = jnp.concatenate([_s, _d, _loop])
        dst = jnp.concatenate([_d, _s, _loop])
        _o = jnp.argsort(dst, stable=True)
        src = src[_o]
        dst = dst[_o]
        edge_type_8 = jax.random.randint(jax.random.fold_in(_gk, 12), (212500,), 0, 8, jnp.int32)
        return (x, src, dst, edge_type_8)
    x, src, dst, edge_type_8 = _rec_inputs()

    def _L0_gnn_setup():
        import jax, jax.numpy as jnp
        import numpy as np
        N_NODES = 6250
        N_EDGES = 100000
        IN_FEAT = 256
        OUT_FEAT = 256
        NUM_RELS = 8
        ALPHA = 0.5
        key = jax.random.key(seed)
        k1, k2, k3, k4, k5, k6 = jax.random.split(key, 6)
        x = jax.random.normal(k1, (N_NODES, IN_FEAT), dtype=jnp.float32)
        edge_index = jax.random.randint(k2, (2, N_EDGES), 0, N_NODES, dtype=jnp.int64)
        edge_type = jax.random.randint(k3, (N_EDGES,), 0, NUM_RELS, dtype=jnp.int64)
        gain = float(np.sqrt(2.0))
        lim_w = gain * float(np.sqrt(6.0 / (IN_FEAT + OUT_FEAT)))
        weight = jax.random.uniform(k4, (NUM_RELS, IN_FEAT, OUT_FEAT), dtype=jnp.float32, minval=-lim_w, maxval=lim_w)
        loop_weight = jax.random.uniform(k5, (IN_FEAT, OUT_FEAT), dtype=jnp.float32, minval=-lim_w, maxval=lim_w)
        h_bias = jnp.zeros((OUT_FEAT,), dtype=jnp.float32)
        return {'edge_index': edge_index, 'x': x, 'edge_type': edge_type, 'weight': weight, 'h_bias': h_bias, 'loop_weight': loop_weight}
    _L0_gnn_all = _L0_gnn_setup()
    _L0_gnn_in = {k: v for k, v in _L0_gnn_all.items() if k in ('weight', 'h_bias', 'loop_weight')}
    del _L0_gnn_all
    return {'x': x, 'src': src, 'dst': dst, 'edge_type_8': edge_type_8, 'L0_gnn_weight': _L0_gnn_in['weight'], 'L0_gnn_h_bias': _L0_gnn_in['h_bias'], 'L0_gnn_loop_weight': _L0_gnn_in['loop_weight']}

def reference(x, src, dst, edge_type_8, L0_gnn_weight, L0_gnn_h_bias, L0_gnn_loop_weight):
    import jax
    import jax.numpy as jnp

    def _L0_gnn_ref(edge_index, x, edge_type, weight, h_bias, loop_weight):
        import jax, jax.numpy as jnp
        import numpy as np
        N_NODES = 6250
        N_EDGES = 100000
        IN_FEAT = 256
        OUT_FEAT = 256
        NUM_RELS = 8
        ALPHA = 0.5
        num_nodes = x.shape[0]
        src, dst = (edge_index[0], edge_index[1])
        hx = jnp.einsum('ni,rio->rno', x, weight)
        msg = hx[edge_type, src]
        agg = jax.ops.segment_sum(msg, dst, num_segments=num_nodes)
        node_repr = agg * jnp.asarray(ALPHA, x.dtype) ** 0.5
        node_repr = node_repr + h_bias
        loop_message = x @ loop_weight
        node_repr = node_repr + loop_message * jnp.asarray(1.0 - ALPHA, x.dtype) ** 0.5
        return node_repr
    edge_index = jnp.stack([src, dst])
    h = jnp.maximum(_layernorm(x, axis=-1), 0.0)
    x = x + _L0_gnn_ref(edge_index, h, edge_type_8, L0_gnn_weight, L0_gnn_h_bias, L0_gnn_loop_weight)
    return x

_drawn_inputs = setup_inputs


def setup_inputs(seed=0):
    import zlib

    import numpy as np

    out = dict(_drawn_inputs(seed))
    spreads = {'L0_gnn_h_bias': (0.0, 0.31)}
    factors = {}
    for name, (base, spread) in spreads.items():
        noise = np.random.default_rng([zlib.crc32(name.encode()), seed]).standard_normal(out[name].shape)
        drawn = base * np.exp(spread * noise) if base else spread * noise
        out[name] = jnp.asarray(drawn.astype(out[name].dtype))
    for name, factor in factors.items():
        out[name] = (out[name] * factor).astype(out[name].dtype)
    return out
```

```python
import concourse.bass as bass
from concourse import mybir
from contextlib import ExitStack


def relational_graph_layer(nc, x, src, dst, etype, weight, h_bias, loop_weight, out, edge_chunks):
    fp32 = mybir.dt.float32
    fp16 = mybir.dt.float16
    i32 = mybir.dt.int32
    ALU = mybir.AluOpType
    ACT = mybir.ActivationFunctionType
    AX = mybir.AxisListType

    P = 128
    N, D = x.shape
    R = weight.shape[0]
    C = dst.shape[1]
    E_CHUNKS = edge_chunks
    TILES = -(-N // P)
    STEPS = TILES
    K = C // STEPS
    K_LAST = E_CHUNKS - (STEPS - 1) * K
    H = D // P
    HR = H * R
    W = P // R
    RING = 4
    SLOT = P + W
    SCALE = 2048.0
    C_OUT = 0.5 ** 0.5 / SCALE
    EPS = 1e-5
    OFFS = -(-K // 4) * 4

    G = 8
    J = N // P // G * G
    LN_GROUPS = J // G
    TAIL = N - P * J
    TJ = 2
    TP = TAIL // TJ

    ONEHOT_GROUPS = [(0, 6), (6, 12), (12, 17)]
    INDEX_GROUPS = [(0, 8), (8, 17)]
    BUFFER_GROUPS = [(0, 4), (4, 8), (8, 12), (12, 17)]

    LAST = N - (TILES - 1) * P

    PITCH = N + 1
    SPILL = R * PITCH
    SUM_ROWS = -(-(SPILL + P) // P) * P
    ZERO_ROWS = P * (HR * SLOT // D)
    ZERO_DMAS = -(-SUM_ROWS // ZERO_ROWS)
    ZEROED = 16 * ZERO_DMAS
    sums_table = nc.dram_tensor("sums_table", (SUM_ROWS, D), fp32, kind="Internal").ap()

    table = nc.dram_tensor("h_table", (N, 2 * D), fp16, kind="Internal").ap()

    ctx = ExitStack()
    with ctx:
        def sb(name, shape, dt):
            return ctx.enter_context(nc.sbuf_tensor(name, shape, dt))

        def pb(name, shape, dt):
            return ctx.enter_context(nc.psum_tensor(name, shape, dt))

        def sem(name):
            return ctx.enter_context(nc.semaphore(name))

        xg = sb("xg", [P, 2, G, D], fp32)
        hg = sb("hg", [P, 2, G, D], fp32)
        tg = sb("tg", [P, 2, G, 2 * D], fp16)
        stats = sb("stats", [P, G, 6], fp32)
        mv = sb("mv", [P, G, 2], fp32)
        rstd = sb("rstd", [P, 2, G], fp32)
        std = sb("std", [P, 2, G], fp32)
        eps = sb("eps", [P, 1], fp32)
        shift = sb("shift", [P, 2, G], fp32)

        src_i = sb("src_i", [P, C], i32)
        dst_i = sb("dst_i", [P, C], i32)
        type_i = sb("type_i", [P, C], i32)
        base_i = sb("base_i", [P, C], i32)
        rel = sb("rel", [P, C], fp32)
        slot = sb("slot", [P, C], fp16)
        step_node = sb("step_node", [P, STEPS], i32)
        tile_of = sb("tile_of", [1, C], i32)
        within = sb("within", [1, C], i32)
        offsets = sb("offsets", [1, STEPS, OFFS], i32)

        lane = sb("lane", [P, P], fp16)
        ident = sb("ident", [P, P], fp16)
        index_now = sb("index_now", [P, K], i32)
        rows = sb("rows", [P, K, 2 * D], fp16)
        onehot = sb("onehot", [P, K, P], fp16)
        ring = sb("ring", [P, HR, RING * SLOT], fp32)
        zeros = sb("zeros", [P, HR, SLOT], fp32)
        carry = sb("carry", [P, HR, W], fp32)

        w_sb = sb("w_sb", [P, H, R + 1, D], fp32)
        bias_b = sb("bias_b", [P, D], fp32)
        stage = sb("stage", [P, HR, P], fp32)
        own = sb("own", [P, 2 * D], fp16)
        own_x = sb("own_x", [P, D], fp32)
        own_hT = sb("own_hT", [P, H, P], fp32)
        result = sb("result", [P, D], fp32)

        unfit_p = sb("unfit_p", [P, 8], fp32)
        unfit_i = sb("unfit_i", [1, 1], i32)
        ones = sb("ones", [P, P], fp32)

        key = rel
        tile_sums = xg[:, 0, :, :]
        ident32 = hg[:, 0, 0, 0:P]
        before = hg[:, 0, 0, P:2 * P]
        spill = hg[:, 0, 1, 0:1]
        duplicate = hg[:, 0, 1, 1:2]
        single = hg[:, 0, 1, 2:3]
        moved = hg[:, 0, 1, 3:4]
        diagonal = hg[:, 0, 2, 0:P]
        masked = hg[:, 0, 2, P:2 * P]
        same = hg[:, 0, 3, 0:P // 2].bitcast(fp16)
        chunk_sum = hg[:, 0, 4, :]
        target = hg[:, 0, 5, 0:1].bitcast(i32)
        zeros_row = zeros[:, :, :].rearrange("p a b -> p (a b)")

        NSUM = 6
        sums = [pb(f"sums{i}", [P, 512], fp32) for i in range(NSUM)]
        ps_out = pb("ps_out", [P, 512], fp32)
        ps_hT = pb("ps_hT", [P, 512], fp32)

        def sum_of(k):
            return sums[k % NSUM][:, 0:HR * W]

        s_x = [sem(f"x_loaded{i}") for i in range(2)]
        s_eps = sem("eps_ready")
        s_var = sem("variance_ready")
        s_std = sem("deviation_ready")
        s_norm = sem("norm_ready")
        s_h = sem("h_ready")
        s_hi = sem("high_ready")
        s_split = sem("split_ready")
        s_tab = [sem(f"table_stored{i}") for i in range(2)]
        s_edges = sem("edges_loaded")
        s_w = sem("weights_loaded")
        s_const = sem("constants_ready")
        s_prep = sem("prep_step")
        s_clear = sem("ring_cleared")
        spill_added = sem("spill_added")
        scaled = sem("product_scaled")
        s_flag = sem("unfit_known")
        s_unfit = sem("unfit_counted")
        s_unfit_sum = sem("unfit_summed")
        g_prep = sem("general_keys_ready")
        g_index = sem("general_index_ready")
        g_rows = sem("general_rows_landed")
        g_diag = sem("general_diagonal_ready")
        g_keys = sem("general_key_row_ready")
        g_same = sem("general_same_ready")
        g_vec = sem("general_vector_step")
        g_target = sem("general_target_ready")
        g_sum = sem("general_sum_ready")
        g_copied = sem("general_sum_copied")
        g_zeroed = sem("general_zeros_in_dram")
        g_added = sem("general_sum_in_dram")
        g_tile = sem("general_tile_landed")
        g_turned = sem("general_tile_transposed")
        index_ready = sem("index_ready")
        landed = [sem(f"rows_landed{k}") for k in range(K)]
        onehot_ready = sem("onehot_ready")
        summed = sem("chunk_summed")
        added = sem("chunk_added")
        carried = sem("tile_carried")
        staged = sem("tile_staged")
        cleared = sem("slot_cleared")
        own_landed = sem("own_rows_landed")
        x_landed = sem("own_x_landed")
        hT_ready = sem("hT_ready")
        hT_copied = sem("hT_copied")
        out_ready = sem("out_ready")
        result_ready = sem("result_ready")
        pool_passed = sem("pool_gates_passed")
        act_passed = sem("scalar_gates_passed")
        stored = sem("result_stored")

        block = ctx.enter_context(nc.Block())

        def group_rows(i):
            return (P, G) if i < LN_GROUPS else (TP, TJ)

        def x_group(i):
            if isinstance(i, int) and i == LN_GROUPS:
                return x[P * J:N].rearrange("(p j) d -> p j d", j=TJ)
            return x[0:P * J].rearrange("(p j) d -> p j d", j=J)[:, bass.ds(i * G, G), :]

        def table_group(i):
            if isinstance(i, int) and i == LN_GROUPS:
                return table[P * J:N].rearrange("(p j) d -> p j d", j=TJ)
            return table[0:P * J].rearrange("(p j) d -> p j d", j=J)[:, bass.ds(i * G, G), :]

        TAB_DONE = [16 * ((LN_GROUPS + 2) // 2), 16 * ((LN_GROUPS + 1) // 2)]

        def pass_gate(engine, passed):
            engine.sem_inc(passed, 1)

        def general_turn(engine, c):
            if isinstance(c, int) and c == 0:
                engine.wait_ge(g_zeroed, ZEROED)
            else:
                engine.wait_ge(g_added, 16 * c)

        def ring_slot(t):
            return t % RING * SLOT

        @block.sync
        def _(sp):
            for i in range(2):
                sp.dma_start(xg[:, i, :, :], x_group(i)).then_inc(s_x[i], 16)
            sp.dma_start(dst_i[:, :], dst).then_inc(s_edges, 16)
            sp.dma_start(base_i[:, :], dst[0:1, :].broadcast_to([P, C])).then_inc(s_edges, 16)
            sp.dma_start(type_i[:, :], etype).then_inc(s_edges, 16)
            sp.dma_start(src_i[:, :], src).then_inc(s_edges, 16)
            for i in range(2, LN_GROUPS + 1):
                n, g = group_rows(i)
                sp.wait_ge(s_h, i - 1)
                sp.dma_start(xg[0:n, i % 2, 0:g, :], x_group(i)).then_inc(s_x[i % 2], 16)
            for h in range(H):
                sp.dma_start(w_sb[:, h, 0:R, :], weight[:, h * P:(h + 1) * P, :].rearrange("r p o -> p r o")
                             ).then_inc(s_w, 16)
                sp.dma_start(w_sb[:, h, R, :], loop_weight[h * P:(h + 1) * P, :]).then_inc(s_w, 16)
            sp.dma_start(bias_b[:, :], h_bias.broadcast_to([P, D])).then_inc(s_w, 16)
            for b in range(2):
                sp.wait_ge(s_tab[b], TAB_DONE[b])

            def own_tile(t, n):
                if not isinstance(t, int) or t > 0:
                    sp.wait_ge(hT_ready, t)
                sp.dma_start(own[0:n, :], table[bass.ds(t * P, n), :]).then_inc(own_landed, 16)

            def own_x_tile(t, n):
                sp.dma_start(own_x[0:n, :], x[bass.ds(t * P, n), :]).then_inc(x_landed, 16)

            def store_tile(t, n):
                sp.wait_ge(result_ready, t + 1)
                sp.dma_start(out[bass.ds(t * P, n), :], result[0:n, :]).then_inc(stored, 16)

            def own_tiles(sums_tile):
                sums_tile(0, P)
                own_tile(0, P)
                own_x_tile(0, P)
                with sp.Fori(0, TILES - 2) as t:
                    sums_tile(t + 1, P)
                    own_tile(t + 1, P)
                    store_tile(t, P)
                    own_x_tile(t + 1, P)
                sums_tile(TILES - 1, LAST)
                own_tile(TILES - 1, LAST)
                store_tile(TILES - 2, P)
                own_x_tile(TILES - 1, LAST)
                store_tile(TILES - 1, LAST)

            def general_tile(t, n):
                if not isinstance(t, int) or t > 0:
                    sp.wait_ge(g_turned, t)
                sp.dma_start(tile_sums[0:n, :, :],
                             sums_table[0:R * PITCH].rearrange("(r n) d -> n r d", r=R)[bass.ds(t * P, n), :, :]
                             ).then_inc(g_tile, 16)

            sp.wait_ge(s_flag, 1)
            unfit = sp.value_load(unfit_i[0:1, 0:1], min_val=0, max_val=1)
            with sp.If(unfit < 1):
                own_tiles(lambda t, n: None)
            with sp.Else():
                for i in range(ZERO_DMAS):
                    a, b = i * ZERO_ROWS, min(SUM_ROWS, (i + 1) * ZERO_ROWS)
                    sp.dma_start(sums_table[a:b, :].rearrange("(p j) d -> p (j d)", p=P),
                                 zeros_row[:, 0:(b - a) // P * D]).then_inc(g_zeroed, 16)
                sp.wait_ge(g_added, 16 * E_CHUNKS)
                own_tiles(general_tile)
            sp.wait_ge(stored, 16 * TILES)

        @block.gpsimd
        def _(pool):
            nc.gpsimd.iota(lane[:, :], [[1, P]], base=0, channel_multiplier=0,
                           allow_small_or_imprecise_dtypes=True)
            nc.gpsimd.iota(step_node[:, :], [[P, STEPS]], base=0, channel_multiplier=0)
            nc.gpsimd.memset(ident[:, :], 0.0).then_inc(s_const, 1)
            pool.wait_ge(s_const, 1)
            nc.gpsimd.affine_select(out=ident[:, :], in_=ident[:, :], compare_op=ALU.not_equal, fill=1.0,
                                    base=0, pattern=[[-1, P]], channel_multiplier=1).then_inc(s_const, 1)
            for i in range(LN_GROUPS + 1):
                n, g = group_rows(i)
                b = i % 2
                pool.wait_ge(s_h, i + 1)
                pool.wait_ge(s_hi, i + 1)
                nc.gpsimd.tensor_tensor(tg[0:n, b, 0:g, D:2 * D], hg[0:n, b, 0:g, :],
                                        tg[0:n, b, 0:g, 0:D], ALU.subtract).then_inc(s_split, 1)
            for b in range(2):
                pool.wait_ge(s_tab[b], TAB_DONE[b])

            def gather_step(s, count):
                for k in range(count):
                    for g, (a, b) in enumerate(INDEX_GROUPS):
                        if k == a:
                            pool.wait_ge(index_ready, len(INDEX_GROUPS) * s + g + 1)
                    for a, b in BUFFER_GROUPS:
                        if k == a:
                            if not isinstance(s, int) or s > 0:
                                pool.wait_ge(summed, K * (s - 1) + b)
                            pass_gate(pool, pool_passed)
                    nc.gpsimd.indirect_dma_start(
                        out=rows[:, k, :], out_offset=None, in_=table[:, :],
                        in_offset=bass.IndirectOffsetOnAxis(ap=index_now[:, k:k + 1], axis=0),
                    ).then_inc(landed[k], 16)

            pool.wait_ge(s_flag, 1)
            unfit = pool.value_load(unfit_i[0:1, 0:1], min_val=0, max_val=1)
            with pool.If(unfit < 1):
                gather_step(0, K)
                with pool.Fori(1, STEPS - 1) as s:
                    gather_step(s, K)
                gather_step(STEPS - 1, K_LAST)
            with pool.Else():
                pool.wait_ge(g_prep, 1)
                nc.gpsimd.memset(ident32, 0.0).then_inc(s_const, 1)
                nc.gpsimd.memset(before, 1.0).then_inc(s_const, 1)
                nc.gpsimd.iota(spill, [[0, 1]], base=SPILL, channel_multiplier=1,
                               allow_small_or_imprecise_dtypes=True).then_inc(s_const, 1)
                pool.wait_ge(s_const, 5)
                nc.gpsimd.affine_select(out=ident32, in_=ident32, compare_op=ALU.not_equal, fill=1.0,
                                        base=0, pattern=[[-1, P]], channel_multiplier=1).then_inc(s_const, 1)
                nc.gpsimd.affine_select(out=before, in_=before, compare_op=ALU.is_gt, fill=0.0,
                                        base=0, pattern=[[-1, P]], channel_multiplier=1).then_inc(s_const, 1)
                with pool.Fori(0, E_CHUNKS) as c:
                    pool.wait_ge(g_index, c + 1)
                    pass_gate(pool, pool_passed)
                    nc.gpsimd.indirect_dma_start(
                        out=rows[:, 0, :], out_offset=None, in_=table[:, :],
                        in_offset=bass.IndirectOffsetOnAxis(ap=index_now[:, 0:1], axis=0)).then_inc(g_rows, 16)
                    pool.wait_ge(g_target, c + 1)
                    pool.wait_ge(g_copied, c + 1)
                    pass_gate(pool, pool_passed)
                    nc.gpsimd.indirect_dma_start(
                        out=sums_table[:, :], out_offset=bass.IndirectOffsetOnAxis(ap=target, axis=0),
                        in_=chunk_sum, in_offset=None, compute_op=ALU.add).then_inc(g_added, 16)
                pool.wait_ge(g_added, 16 * E_CHUNKS)

        @block.scalar
        def _(act):
            act.wait_ge(s_eps, 1)
            for i in range(LN_GROUPS + 1):
                n, g = group_rows(i)
                b = i % 2
                act.wait_ge(s_var, i + 1)
                nc.scalar.activation(std[0:n, b, 0:g], mv[0:n, 0:g, 1], ACT.Sqrt, bias=eps[0:n, :],
                                     scale=SCALE ** -2).then_inc(s_std, 1)
                act.wait_ge(s_norm, i + 1)
                act.wait_ge(s_x[b], 16 * (i // 2 + 1))
                if i >= 2:
                    act.wait_ge(s_split, i - 1)
                for j in range(g):
                    last = nc.scalar.activation(hg[0:n, b, j, :], xg[0:n, b, j, :], ACT.Relu,
                                                bias=shift[0:n, b, j:j + 1], scale=rstd[0:n, b, j:j + 1])
                last.then_inc(s_h, 1)
                if i >= 2:
                    act.wait_ge(s_tab[b], 16 * (i // 2))
                act.wait_ge(s_h, i + 1)
                nc.scalar.copy(tg[0:n, b, 0:g, 0:D], hg[0:n, b, 0:g, :]).then_inc(s_hi, 1)
                if i >= 1:
                    m, q = group_rows(i - 1)
                    act.wait_ge(s_split, i)
                    act.dma_start(table_group(i - 1), tg[0:m, (i - 1) % 2, 0:q, :]).then_inc(s_tab[(i - 1) % 2], 16)
            act.wait_ge(s_split, LN_GROUPS + 1)
            act.dma_start(table_group(LN_GROUPS), tg[0:TP, LN_GROUPS % 2, 0:TJ, :]).then_inc(s_tab[LN_GROUPS % 2], 16)

            def index_group(s, g):
                a, b = INDEX_GROUPS[g]
                nc.scalar.copy(index_now[:, a:b], src_i[:, bass.ds(s * K + a, b - a)]).then_inc(index_ready, 1)

            def stage_tile(t):
                act.wait_ge(carried, t + 1)
                if not isinstance(t, int) or t > 0:
                    act.wait_ge(out_ready, t)
                pass_gate(act, act_passed)
                nc.scalar.copy(stage[:, :, :], ring[:, :, bass.ds(ring_slot(t), P)]).then_inc(staged, 1)
                act.wait_ge(staged, t + 1)
                pass_gate(act, act_passed)
                nc.scalar.copy(ring[:, :, bass.ds(ring_slot(t), SLOT)], zeros[:, :, :]).then_inc(cleared, 1)

            def copy_hT(t):
                act.wait_ge(hT_ready, t + 1)
                nc.scalar.copy(own_hT[:, :, :], ps_hT[:, 0:D].rearrange("p (h n) -> p h n", h=H)
                               ).then_inc(hT_copied, 1)

            def scalar_step(s, finish, ahead):
                if finish:
                    stage_tile(s - 2)
                for g in range(2):
                    if ahead:
                        act.wait_ge(summed, K * s + INDEX_GROUPS[g][1])
                        pass_gate(act, act_passed)
                        index_group(s + 1, g)
                    if finish and g == 0:
                        copy_hT(s - 2)

            def general_chunk(c):
                general_turn(act, c)
                pass_gate(act, act_passed)
                nc.scalar.copy(index_now[:, 0:1], src_i[:, bass.ds(c, 1)]).then_inc(g_index, 1)
                act.wait_ge(g_sum, c + 1)
                nc.scalar.copy(chunk_sum, ps_out[:, 0:D]).then_inc(g_copied, 1)

            def general_stage(t):
                act.wait_ge(g_turned, t + 1)
                if not isinstance(t, int) or t > 0:
                    act.wait_ge(out_ready, t)
                for q in range(HR // 4):
                    last = nc.scalar.copy(stage[:, 4 * q:4 * q + 4, :],
                                          sums[q][:, :].rearrange("p (a n) -> p a n", a=4))
                last.then_inc(staged, 1)
                copy_hT(t)

            act.wait_ge(s_clear, 2)
            act.wait_ge(s_edges, 16 * 4)
            act.wait_ge(s_flag, 1)
            unfit = act.value_load(unfit_i[0:1, 0:1], min_val=0, max_val=1)
            with act.If(unfit < 1):
                for g in range(2):
                    index_group(0, g)
                for s in range(3):
                    scalar_step(s, s >= 2, True)
                with act.Fori(3, STEPS - 1) as s:
                    scalar_step(s, True, True)
                for s in range(STEPS - 1, STEPS + 2):
                    scalar_step(s, True, False)
            with act.Else():
                general_chunk(0)
                with act.Fori(1, E_CHUNKS) as c:
                    general_chunk(c)
                general_stage(0)
                with act.Fori(1, TILES) as t:
                    general_stage(t)

        @block.vector
        def _(dve):
            nc.vector.memset(eps[:, :], EPS * SCALE ** -2).then_inc(s_eps, 1)
            nc.vector.memset(ring[:, :, :], 0.0).then_inc(s_clear, 1)
            nc.vector.memset(zeros[:, :, :], 0.0).then_inc(s_clear, 1)
            nc.vector.memset(carry[:, :, :], 0.0).then_inc(s_clear, 1)
            steps = [0]

            def link(ins):
                steps[0] += 1
                ins.then_inc(s_prep, 1)
                dve.wait_ge(s_prep, steps[0])

            for i in range(LN_GROUPS + 1):
                n, g = group_rows(i)
                b = i % 2
                dve.wait_ge(s_x[b], 16 * (i // 2 + 1))
                for j in range(g):
                    last = nc.vector.bn_stats(stats[0:n, j, :], xg[0:n, b, j, :])
                link(last)
                if i >= 1:
                    dve.wait_ge(s_std, i)
                for j in range(g):
                    last = nc.vector.bn_aggr(mv[0:n, j, :], stats[0:n, j, :])
                last.then_inc(s_var, 1)
                dve.wait_ge(s_var, i + 1)
                if i >= 2:
                    dve.wait_ge(s_h, i - 1)
                dve.wait_ge(s_std, i + 1)
                link(nc.vector.reciprocal(rstd[0:n, b, 0:g], std[0:n, b, 0:g]))
                nc.vector.scalar_tensor_tensor(shift[0:n, b, 0:g], mv[0:n, 0:g, 0], -1.0, rstd[0:n, b, 0:g],
                                               ALU.mult, ALU.mult).then_inc(s_norm, 1)

            dve.wait_ge(s_edges, 16 * 4)
            link(nc.vector.tensor_tensor(rel[:, :], dst_i[:, :], base_i[:, :], ALU.subtract))
            nc.vector.scalar_tensor_tensor(slot[:, :], type_i[:, :], float(W), rel[:, :], ALU.mult, ALU.add)
            nc.vector.tensor_scalar(tile_of[:, :], base_i[0:1, :], 7, RING - 1, ALU.arith_shift_right, ALU.bitwise_and)
            link(nc.vector.tensor_scalar(within[:, :], base_i[0:1, :], P - 1, None, ALU.bitwise_and))
            dve.wait_ge(s_const, 2)
            link(nc.vector.scalar_tensor_tensor(
                offsets[:, :, 0:K], tile_of[:, :].rearrange("p (s k) -> p s k", k=K), float(SLOT),
                within[:, :].rearrange("p (s k) -> p s k", k=K), ALU.mult, ALU.add))

            ahead_of = hg[:, :, :, :].rearrange("p b g d -> p (b g d)")[:, 0:C]
            dve.wait_ge(s_split, LN_GROUPS + 1)
            link(nc.vector.tensor_tensor(
                ahead_of.rearrange("p (s k) -> p s k", k=K), base_i[:, :].rearrange("p (s k) -> p s k", k=K),
                step_node[:, :].unsqueeze(2).broadcast_to([P, STEPS, K]), ALU.subtract))
            nc.vector.tensor_reduce(unfit_p[:, 0:1], rel[:, :], AX.X, ALU.max)
            nc.vector.tensor_reduce(unfit_p[:, 1:2], rel[:, :], AX.X, ALU.min)
            nc.vector.tensor_reduce(unfit_p[:, 2:3], ahead_of, AX.X, ALU.max)
            link(nc.vector.tensor_reduce(unfit_p[:, 3:4], ahead_of, AX.X, ALU.min))
            nc.vector.tensor_scalar(unfit_p[:, 4:5], unfit_p[:, 0:1], float(W - 1), None, ALU.is_gt)
            nc.vector.tensor_scalar(unfit_p[:, 5:6], unfit_p[:, 1:2], 0.0, None, ALU.is_lt)
            nc.vector.tensor_scalar(unfit_p[:, 6:7], unfit_p[:, 2:3], float(2 * P - W), None, ALU.is_gt)
            nc.vector.tensor_scalar(unfit_p[:, 7:8], unfit_p[:, 3:4], float(-P), None, ALU.is_lt)
            nc.vector.memset(ones[:, :], 1.0).then_inc(s_unfit, 1)
            dve.wait_ge(s_unfit_sum, 1)
            nc.vector.tensor_reduce(unfit_p[0:1, 0:1], ps_out[0:1, 0:4], AX.X, ALU.add).then_inc(s_unfit, 1)
            dve.wait_ge(s_unfit, 2)
            nc.vector.tensor_scalar(unfit_i[:, :], unfit_p[0:1, 0:1], 0.5, None, ALU.is_gt).then_inc(s_flag, 1)

            dve.wait_ge(s_const, 2)

            def onehot_group(s, g, count=K):
                a, b = ONEHOT_GROUPS[g]
                b = min(b, count)
                if b > a:
                    nc.vector.tensor_tensor(
                        onehot[:, a:b, :], lane[:, :].unsqueeze(1).broadcast_to([P, b - a, P]),
                        slot[:, bass.ds(s * K + a, b - a)].unsqueeze(2).broadcast_to([P, b - a, P]),
                        ALU.is_equal).then_inc(onehot_ready, 1)

            dve.wait_ge(s_clear, 3)

            def carry_tile(t):
                head = ring[:, :, bass.ds(ring_slot(t), W)]
                if not isinstance(t, int) or t > 0:
                    dve.wait_ge(carried, t)
                nc.vector.tensor_tensor(head, head, carry[:, :, :], ALU.add).then_inc(spill_added, 1)
                dve.wait_ge(spill_added, t + 1)
                nc.vector.tensor_copy(carry[:, :, :], ring[:, :, bass.ds(ring_slot(t) + P, W)]
                                      ).then_inc(carried, 1)

            def finish_tile(t, n):
                dve.wait_ge(out_ready, t + 1)
                dve.wait_ge(x_landed, 16 * (t + 1))
                if not isinstance(t, int) or t > 0:
                    dve.wait_ge(stored, 16 * t)
                nc.vector.scalar_tensor_tensor(result[0:n, :], ps_out[0:n, 0:D], C_OUT, own_x[0:n, :],
                                               ALU.mult, ALU.add).then_inc(scaled, 1)
                dve.wait_ge(scaled, t + 1)
                nc.vector.tensor_tensor(result[0:n, :], result[0:n, :], bias_b[0:n, :], ALU.add
                                        ).then_inc(result_ready, 1)

            def vector_step(s, count, closes, finish, ahead, ahead_count=K):
                for k in range(count):
                    if k % 4 == 0:
                        m = min(4, count - k)
                        _, offs = nc.values_load_multi_w_load_instructions(
                            offsets[0:1, bass.ds(s, 1), k:k + m].rearrange("p s k -> p (s k)"),
                            engines=[mybir.EngineType.DVE], min_val=0, max_val=RING * SLOT - W,
                            skip_runtime_bounds_check_because="offset = tile % RING * SLOT + node % P, "
                            "whatever the node, and P - 1 + W < SLOT + 1")
                    if k == 0 and (not isinstance(s, int) or s > 2):
                        dve.wait_ge(cleared, s - 2)
                    dve.wait_ge(summed, K * s + k + 1)
                    if not isinstance(s, int) or s > 0 or k > 0:
                        dve.wait_ge(added, K * s + k)
                    window = ring[:, :, bass.ds(offs[k % 4], W)]
                    nc.vector.tensor_tensor(window, window, sum_of(k).rearrange("p (a w) -> p a w", w=W),
                                            ALU.add).then_inc(added, 1)
                    for g, (a, b) in enumerate(ONEHOT_GROUPS):
                        if ahead and k == b - 1:
                            onehot_group(s + 1, g, ahead_count)
                if closes:
                    carry_tile(s - 1)
                if finish:
                    finish_tile(s - 2, P)

            def general_chunk(c):
                def done(i):
                    return 6 * c + i

                general_turn(dve, c)
                now = key[:, bass.ds(c, 1)]
                nc.vector.tensor_scalar(diagonal, ident32, now, None, ALU.mult).then_inc(g_diag, 1)
                dve.wait_ge(g_keys, c + 1)
                nc.vector.tensor_scalar(same, ps_hT[:, 0:P], now, None, ALU.is_equal).then_inc(g_same, 1)
                dve.wait_ge(g_same, c + 1)
                nc.vector.tensor_tensor(masked, same, before, ALU.mult).then_inc(g_vec, 1)
                dve.wait_ge(g_vec, done(1))
                nc.vector.tensor_reduce(duplicate, masked, AX.X, ALU.max).then_inc(g_vec, 1)
                dve.wait_ge(g_vec, done(2))
                nc.vector.tensor_scalar(single, duplicate, -1.0, 1.0, ALU.mult, ALU.add).then_inc(g_vec, 1)
                nc.vector.tensor_tensor(moved, now, spill, ALU.subtract).then_inc(g_vec, 1)
                dve.wait_ge(g_vec, done(4))
                nc.vector.tensor_tensor(moved, moved, single, ALU.mult).then_inc(g_vec, 1)
                dve.wait_ge(g_vec, done(5))
                nc.vector.tensor_tensor(target, moved, spill, ALU.add).then_inc(g_vec, 1)
                dve.wait_ge(g_vec, done(6))
                dve.sem_inc(g_target, 1)

            dve.wait_ge(s_w, 16 * (2 * H + 1))
            dve.wait_ge(s_flag, 1)
            unfit = dve.value_load(unfit_i[0:1, 0:1], min_val=0, max_val=1)
            with dve.If(unfit < 1):
                for g in range(len(ONEHOT_GROUPS)):
                    onehot_group(0, g)
                for s in range(3):
                    vector_step(s, K, s >= 1, s >= 2, True)
                with dve.Fori(3, STEPS - 2) as s:
                    vector_step(s, K, True, True, True)
                vector_step(STEPS - 2, K, True, True, True, K_LAST)
                vector_step(STEPS - 1, K_LAST, True, True, False)
                finish_tile(TILES - 2, P)
                carry_tile(TILES - 1)
                finish_tile(TILES - 1, LAST)
            with dve.Else():
                dve.wait_ge(s_tab[0], TAB_DONE[0])
                dve.wait_ge(s_tab[1], TAB_DONE[1])
                nc.vector.scalar_tensor_tensor(key[:, :], type_i[:, :], float(PITCH), dst_i[:, :],
                                               ALU.mult, ALU.add).then_inc(g_prep, 1)
                dve.wait_ge(g_prep, 1)
                dve.wait_ge(s_const, 7)
                general_chunk(0)
                with dve.Fori(1, E_CHUNKS) as c:
                    general_chunk(c)
                finish_tile(0, P)
                with dve.Fori(1, TILES - 1) as t:
                    finish_tile(t, P)
                finish_tile(TILES - 1, LAST)

        @block.tensor
        def _(pe):
            pe.wait_ge(s_const, 2)
            pe.wait_ge(s_w, 16 * (2 * H + 1))

            def own_rows(t):
                pe.wait_ge(own_landed, 16 * (t + 1))
                if not isinstance(t, int) or t > 0:
                    pe.wait_ge(hT_copied, t)
                for h in range(H):
                    for part in range(2):
                        last = nc.tensor.matmul(ps_hT[:, h * P:(h + 1) * P],
                                                own[:, part * D + h * P:part * D + (h + 1) * P], ident[:, :],
                                                start=(part == 0), stop=(part == 1))
                last.then_inc(hT_ready, 1)

            def tile_product(t, m):
                if m == 0:
                    pe.wait_ge(staged, t + 1)
                    if not isinstance(t, int) or t > 0:
                        pe.wait_ge(result_ready, t)
                if m < HR:
                    h, r = m // R, m % R
                    nc.tensor.matmul(ps_out[:, 0:D], stage[:, m, :], w_sb[:, h, r, :], start=(m == 0), stop=False)
                else:
                    h = m - HR
                    if h == 0:
                        pe.wait_ge(hT_copied, t + 1)
                    last = nc.tensor.matmul(ps_out[:, 0:D], own_hT[:, h, :], w_sb[:, h, R, :],
                                            start=False, stop=(h == H - 1))
                    if h == H - 1:
                        last.then_inc(out_ready, 1)

            def tensor_step(s, count, finish):
                products = list(range(HR + H)) if finish else []
                for k in range(count):
                    for g, (a, b) in enumerate(ONEHOT_GROUPS):
                        if k == a:
                            pe.wait_ge(onehot_ready, len(ONEHOT_GROUPS) * s + g + 1)
                    if not isinstance(s, int) or s > 0:
                        pe.wait_ge(landed[k], 16 * (s + 1))
                        pe.wait_ge(added, K * s + k - NSUM + 1 if k >= NSUM
                                   else K * (s - 1) + (k + 12 - NSUM * (k > 4)) + 1)
                    else:
                        pe.wait_ge(landed[k], 16)
                        if k >= NSUM:
                            pe.wait_ge(added, k - NSUM + 1)
                    for h in range(H):
                        for part in range(2):
                            last = nc.tensor.matmul(sum_of(k)[:, h * P:(h + 1) * P],
                                                    rows[:, k, part * D + h * P:part * D + (h + 1) * P],
                                                    onehot[:, k, :], start=(part == 0), stop=(part == 1))
                    last.then_inc(summed, 1)
                    if finish and k == 3:
                        own_rows(s - 2)
                    if k >= 8:
                        now = 2 if len(products) > count - 2 - k else 1
                        for m in products[:now]:
                            tile_product(s - 2, m)
                        products = products[now:]
                for m in products:
                    tile_product(s - 2, m)

            def whole_tile(t):
                own_rows(t)
                for m in range(HR + H):
                    tile_product(t, m)

            def general_chunk(c):
                pe.wait_ge(g_diag, c + 1)
                nc.tensor.matmul(ps_hT[:, 0:P], ones[:, :], diagonal, start=True, stop=True).then_inc(g_keys, 1)
                pe.wait_ge(g_same, c + 1)
                pe.wait_ge(g_rows, 16 * (c + 1))
                nc.tensor.matmul(ps_out[:, 0:D], same, rows[:, 0, 0:D], start=True, stop=False)
                nc.tensor.matmul(ps_out[:, 0:D], same, rows[:, 0, D:2 * D], start=False, stop=True
                                 ).then_inc(g_sum, 1)

            def general_tile(t):
                pe.wait_ge(g_tile, 16 * (t + 1))
                if not isinstance(t, int) or t > 0:
                    pe.wait_ge(staged, t)
                for m in range(HR):
                    h, r = m // R, m % R
                    last = nc.tensor.matmul(sums[m // 4][:, m % 4 * P:(m % 4 + 1) * P],
                                            tile_sums[:, r, h * P:(h + 1) * P], ident32, start=True, stop=True)
                last.then_inc(g_turned, 1)
                whole_tile(t)

            pe.wait_ge(s_unfit, 1)
            nc.tensor.matmul(ps_out[0:1, 0:4], ones[:, 0:1], unfit_p[:, 4:8], start=True, stop=True
                             ).then_inc(s_unfit_sum, 1)
            pe.wait_ge(s_flag, 1)
            unfit = pe.value_load(unfit_i[0:1, 0:1], min_val=0, max_val=1)
            with pe.If(unfit < 1):
                for s in range(3):
                    tensor_step(s, K, s >= 2)
                with pe.Fori(3, STEPS - 1) as s:
                    tensor_step(s, K, True)
                tensor_step(STEPS - 1, K_LAST, True)
                for t in range(TILES - 2, TILES):
                    whole_tile(t)
            with pe.Else():
                pe.wait_ge(s_const, 7)
                with pe.Fori(0, E_CHUNKS) as c:
                    general_chunk(c)
                pe.wait_ge(g_copied, E_CHUNKS)
                general_tile(0)
                with pe.Fori(1, TILES) as t:
                    general_tile(t)


def kernel(x, src, dst, edge_type_8, L0_gnn_weight, L0_gnn_h_bias, L0_gnn_loop_weight):
    import numpy as np
    import concourse.bacc as bacc
    from concourse.bass_utils import run_bass_kernel_spmd as run

    P = 128
    n, d = x.shape
    edges = src.shape[0]
    tiles = -(-n // P)
    chunks = -(-edges // P)
    padded = -(-chunks // tiles) * tiles

    def by_chunk(a, fill):
        flat = np.full(padded * P, fill, np.int32)
        flat[:edges] = np.asarray(a)
        return np.ascontiguousarray(flat.reshape(padded, P).T)

    arrays = {
        "x": np.ascontiguousarray(x),
        "src": by_chunk(src, 0),
        "dst": by_chunk(dst, n),
        "etype": by_chunk(edge_type_8, 0),
        "weight": np.ascontiguousarray(L0_gnn_weight),
        "h_bias": np.ascontiguousarray(L0_gnn_h_bias).reshape(1, d),
        "loop_weight": np.ascontiguousarray(L0_gnn_loop_weight),
    }
    nc = bacc.Bacc("TRN2", target_bir_lowering=False, num_devices=1)
    args = [nc.dram_tensor(k, a.shape, mybir.dt.from_np(a.dtype), kind="ExternalInput").ap() for k, a in arrays.items()]
    out = nc.dram_tensor("out", (n, d), mybir.dt.float32, kind="ExternalOutput").ap()
    relational_graph_layer(nc, *args, out, chunks)
    return run(nc, [arrays], core_ids=[0]).results[0]["out"]
```

```python
import concourse.bass as bass
from concourse import mybir
from contextlib import ExitStack


def relational_graph_layer(nc, x, src, dst, etype, weight, h_bias, loop_weight, out, edge_chunks):
    fp32 = mybir.dt.float32
    fp16 = mybir.dt.float16
    i32 = mybir.dt.int32
    ALU = mybir.AluOpType
    ACT = mybir.ActivationFunctionType
    AX = mybir.AxisListType

    P = 128
    N, D = x.shape
    R = weight.shape[0]
    C = dst.shape[1]
    E_CHUNKS = edge_chunks
    TILES = -(-N // P)
    STEPS = TILES
    K = C // STEPS
    K_LAST = E_CHUNKS - (STEPS - 1) * K
    H = D // P
    HR = H * R
    W = P // R
    RING = 4
    SLOT = P + W
    SCALE = 2048.0
    C_OUT = 0.5 ** 0.5 / SCALE
    EPS = 1e-5
    HALF = 0.5 / SCALE
    OFFS = -(-K // 4) * 4

    G = 8
    J = N // P // G * G
    LN_GROUPS = J // G
    TAIL = N - P * J
    TJ = 2
    TP = TAIL // TJ
    XB = 3
    GV = 3

    ONEHOT_GROUPS = [(a, min(a + 6, K)) for a in range(0, K, 6)]
    INDEX_GROUPS = [(0, K // 2), (K // 2, K)]
    BUFFER_GROUPS = [(0, K // 4), (K // 4, K // 2), (K // 2, K // 4 * 3), (K // 4 * 3, K)]

    LAST = N - (TILES - 1) * P

    PITCH = N + 1
    SPILL = R * PITCH
    SUM_ROWS = -(-(SPILL + P) // P) * P
    ZERO_ROWS = P * (HR * SLOT // D)
    ZERO_DMAS = -(-SUM_ROWS // ZERO_ROWS)
    ZEROED = 16 * ZERO_DMAS
    sums_table = nc.dram_tensor("sums_table", (SUM_ROWS, D), fp32, kind="Internal").ap()

    table = nc.dram_tensor("h_table", (N, 2 * D), fp16, kind="Internal").ap()

    ctx = ExitStack()
    with ctx:
        def sb(name, shape, dt):
            return ctx.enter_context(nc.sbuf_tensor(name, shape, dt))

        def pb(name, shape, dt):
            return ctx.enter_context(nc.psum_tensor(name, shape, dt))

        def sem(name):
            return ctx.enter_context(nc.semaphore(name))

        xg = sb("xg", [P, XB, G, D], fp32)
        hg = sb("hg", [P, 2, G, D], fp32)
        tg = sb("tg", [P, 2, G, 2 * D], fp16)
        stats = sb("stats", [P, G, 6], fp32)
        mv = sb("mv", [P, 2, G, 2], fp32)
        rstd = sb("rstd", [P, 2, G], fp32)
        std = sb("std", [P, 2, G], fp32)
        eps = sb("eps", [P, 1], fp32)
        root = sb("root", [P, G], fp32)
        shift = sb("shift", [P, 2, G], fp32)

        src_i = sb("src_i", [P, C], i32)
        dst_i = sb("dst_i", [P, C], i32)
        type_i = sb("type_i", [P, C], i32)
        base_i = sb("base_i", [P, C], i32)
        rel = sb("rel", [P, C], i32)
        slot = sb("slot", [P, C], fp16)
        step_node = sb("step_node", [P, STEPS], i32)
        offsets = sb("offsets", [1, STEPS, OFFS], i32)

        lane = sb("lane", [P, P], fp16)
        ident = sb("ident", [P, P], fp16)
        index_now = sb("index_now", [P, K], i32)
        rows = sb("rows", [P, K, 2 * D], fp16)
        onehot = sb("onehot", [P, K, P], fp16)
        ring = sb("ring", [P, HR, RING * SLOT], fp32)
        zeros = sb("zeros", [P, HR, SLOT], fp32)
        carry = sb("carry", [P, HR, W], fp32)

        w_sb = sb("w_sb", [P, H, R + 1, D], fp32)
        bias_b = sb("bias_b", [P, D], fp32)
        stage = sb("stage", [P, HR, P], fp32)
        own = sb("own", [P, 2 * D], fp16)
        own_x = sb("own_x", [P, D], fp32)
        own_hT = sb("own_hT", [P, H, P], fp32)
        result = sb("result", [P, D], fp32)

        unfit_p = sb("unfit_p", [P, 8], fp32)
        unfit_i = sb("unfit_i", [1, 1], i32)
        ones = sb("ones", [P, P], fp32)

        key = rel[:, :].bitcast(fp32)
        tile_sums = xg[:, 0, :, :]
        ident32 = hg[:, 0, 0, 0:P]
        before = hg[:, 0, 0, P:2 * P]
        spill = hg[:, 0, 1, 0:1]
        duplicate = hg[:, 0, 1, 1:2]
        single = hg[:, 0, 1, 2:3]
        moved = hg[:, 0, 1, 3:4]
        diagonal = hg[:, 0, 2, 0:P]
        masked = hg[:, 0, 2, P:2 * P]
        same = hg[:, 0, 3, 0:P // 2].bitcast(fp16)
        chunk_sum = hg[:, 0, 4, :]
        target = hg[:, 0, 5, 0:1].bitcast(i32)
        zeros_row = zeros[:, :, :].rearrange("p a b -> p (a b)")

        rows_room = rows[:, :, :].rearrange("p k d -> p (k d)").bitcast(fp32)
        ahead_of = rows_room[:, 0:C].bitcast(i32)
        tile_of = rows_room[0:1, C:2 * C].bitcast(i32)
        within = stage[0:1, :, :].rearrange("p a n -> p (a n)").bitcast(i32)[:, 0:C]

        last_stage = xg[:, 1, :, :].rearrange("p g d -> p (g d)").rearrange("p (a n) -> p a n", a=HR)
        last_hT = xg[:, 2, 0, :].rearrange("p (h n) -> p h n", h=H)

        NSUM = 6
        sums = [pb(f"sums{i}", [P, 512], fp32) for i in range(NSUM)]
        ps_out = pb("ps_out", [P, 512], fp32)
        ps_hT = pb("ps_hT", [P, 512], fp32)

        last_out = sums[0]

        def sum_of(k):
            return sums[k % NSUM][:, 0:HR * W]

        s_x = [sem(f"x_loaded{i}") for i in range(XB)]
        s_eps = sem("eps_ready")
        s_var = sem("variance_ready")
        s_std = sem("deviation_ready")
        s_scale = sem("scale_ready")
        s_norm = sem("vector_rows_scaled")
        s_norm_act = sem("scalar_rows_scaled")
        s_h = sem("h_ready")
        s_hi = sem("high_ready")
        s_split = sem("split_ready")
        s_tab = [sem(f"table_stored{i}") for i in range(2)]
        s_nodes = sem("edges_nodes_loaded")
        s_src = sem("edges_sources_loaded")
        s_types = sem("edges_types_loaded")
        s_w = sem("weights_loaded")
        s_const = sem("constants_ready")
        s_prep = sem("prep_step")
        s_zeros = sem("zeros_ready")
        s_places = sem("edges_places_ready")
        s_window = sem("window_step")
        s_slot = sem("slots_ready")
        spill_added = sem("spill_added")
        scaled = sem("product_scaled")
        s_flag = sem("unfit_known")
        s_unfit = sem("unfit_counted")
        s_unfit_sum = sem("unfit_summed")
        g_prep = sem("general_keys_ready")
        g_index = sem("general_index_ready")
        g_rows = sem("general_rows_landed")
        g_diag = sem("general_diagonal_ready")
        g_keys = sem("general_key_row_ready")
        g_same = sem("general_same_ready")
        g_vec = sem("general_vector_step")
        g_target = sem("general_target_ready")
        g_sum = sem("general_sum_ready")
        g_copied = sem("general_sum_copied")
        g_zeroed = sem("general_zeros_in_dram")
        g_added = sem("general_sum_in_dram")
        g_tile = sem("general_tile_landed")
        g_turned = sem("general_tile_transposed")
        index_ready = sem("index_ready")
        landed = [sem(f"rows_landed{k}") for k in range(K)]
        onehot_ready = sem("onehot_ready")
        summed = sem("chunk_summed")
        added = sem("chunk_added")
        carried = sem("tile_carried")
        staged = sem("tile_staged")
        last_staged = sem("last_tiles_staged")
        cleared = sem("slot_cleared")
        own_landed = sem("own_rows_landed")
        x_landed = sem("own_x_landed")
        hT_ready = sem("hT_ready")
        hT_copied = sem("hT_copied")
        out_ready = sem("out_ready")
        result_ready = sem("result_ready")
        pool_passed = sem("pool_gates_passed")
        act_passed = sem("scalar_gates_passed")
        stored = sem("result_stored")

        block = ctx.enter_context(nc.Block())

        def group_rows(i):
            return (P, G) if i < LN_GROUPS else (TP, TJ)

        def x_group(i):
            if isinstance(i, int) and i == LN_GROUPS:
                return x[P * J:N].rearrange("(p j) d -> p j d", j=TJ)
            return x[0:P * J].rearrange("(p j) d -> p j d", j=J)[:, bass.ds(i * G, G), :]

        def table_group(i):
            if isinstance(i, int) and i == LN_GROUPS:
                return table[P * J:N].rearrange("(p j) d -> p j d", j=TJ)
            return table[0:P * J].rearrange("(p j) d -> p j d", j=J)[:, bass.ds(i * G, G), :]

        TAB_DONE = [16 * ((LN_GROUPS + 2) // 2), 16 * ((LN_GROUPS + 1) // 2)]

        def pass_gate(engine, passed):
            engine.sem_inc(passed, 1)

        def general_turn(engine, c):
            if isinstance(c, int) and c == 0:
                engine.wait_ge(g_zeroed, ZEROED)
            else:
                engine.wait_ge(g_added, 16 * c)

        def ring_slot(t):
            return t % RING * SLOT

        @block.sync
        def _(sp):
            for i in range(LN_GROUPS + 1):
                n, g = group_rows(i)
                if i >= XB:
                    sp.wait_ge(s_norm, i - XB + 1)
                    sp.wait_ge(s_norm_act, i - XB + 1)
                sp.dma_start(xg[0:n, i % XB, 0:g, :], x_group(i)).then_inc(s_x[i % XB], 16)
                if i == XB - 1:
                    sp.dma_start(dst_i[:, :], dst).then_inc(s_nodes, 16)
                    sp.dma_start(base_i[:, :], dst[0:1, :].broadcast_to([P, C])).then_inc(s_nodes, 16)
                if i == 5:
                    sp.dma_start(type_i[:, :], etype).then_inc(s_types, 16)
                if i == 7:
                    sp.dma_start(src_i[:, :], src).then_inc(s_src, 16)
            for b in range(2):
                sp.wait_ge(s_tab[b], TAB_DONE[b])
            for h in range(H):
                sp.dma_start(w_sb[:, h, 0:R, :], weight[:, h * P:(h + 1) * P, :].rearrange("r p o -> p r o")
                             ).then_inc(s_w, 16)
                sp.dma_start(w_sb[:, h, R, :], loop_weight[h * P:(h + 1) * P, :]).then_inc(s_w, 16)
            sp.dma_start(bias_b[:, :], h_bias.broadcast_to([P, D])).then_inc(s_w, 16)

            def own_tile(t, n):
                if not isinstance(t, int) or t > 0:
                    sp.wait_ge(hT_ready, t)
                sp.dma_start(own[0:n, :], table[bass.ds(t * P, n), :]).then_inc(own_landed, 16)

            def own_x_tile(t, n):
                sp.dma_start(own_x[0:n, :], x[bass.ds(t * P, n), :]).then_inc(x_landed, 16)

            def store_tile(t, n):
                sp.wait_ge(result_ready, t + 1)
                sp.dma_start(out[bass.ds(t * P, n), :], result[0:n, :]).then_inc(stored, 16)

            def own_tiles(sums_tile):
                sums_tile(0, P)
                own_tile(0, P)
                own_x_tile(0, P)
                with sp.Fori(0, TILES - 2) as t:
                    sums_tile(t + 1, P)
                    own_tile(t + 1, P)
                    store_tile(t, P)
                    own_x_tile(t + 1, P)
                sums_tile(TILES - 1, LAST)
                own_tile(TILES - 1, LAST)
                store_tile(TILES - 2, P)
                own_x_tile(TILES - 1, LAST)
                store_tile(TILES - 1, LAST)

            def general_tile(t, n):
                if not isinstance(t, int) or t > 0:
                    sp.wait_ge(g_turned, t)
                sp.dma_start(tile_sums[0:n, :, :],
                             sums_table[0:R * PITCH].rearrange("(r n) d -> n r d", r=R)[bass.ds(t * P, n), :, :]
                             ).then_inc(g_tile, 16)

            sp.wait_ge(s_flag, 1)
            unfit = sp.value_load(unfit_i[0:1, 0:1], min_val=0, max_val=1)
            with sp.If(unfit < 1):
                own_tiles(lambda t, n: None)
            with sp.Else():
                sp.wait_ge(s_zeros, 1)
                for i in range(ZERO_DMAS):
                    a, b = i * ZERO_ROWS, min(SUM_ROWS, (i + 1) * ZERO_ROWS)
                    sp.dma_start(sums_table[a:b, :].rearrange("(p j) d -> p (j d)", p=P),
                                 zeros_row[:, 0:(b - a) // P * D]).then_inc(g_zeroed, 16)
                sp.wait_ge(g_added, 16 * E_CHUNKS)
                own_tiles(general_tile)
            sp.wait_ge(stored, 16 * TILES)

        @block.gpsimd
        def _(pool):
            nc.gpsimd.iota(lane[:, :], [[1, P]], base=0, channel_multiplier=0,
                           allow_small_or_imprecise_dtypes=True)
            nc.gpsimd.iota(step_node[:, :], [[P, STEPS]], base=0, channel_multiplier=0)
            nc.gpsimd.memset(ident[:, :], 0.0).then_inc(s_const, 1)
            nc.gpsimd.memset(zeros[:, :, :], 0.0).then_inc(s_zeros, 1)
            nc.gpsimd.memset(carry[:, :, :], 0.0).then_inc(s_zeros, 1)
            nc.gpsimd.memset(ring[:, :, :], 0.0).then_inc(s_zeros, 1)
            pool.wait_ge(s_const, 1)
            nc.gpsimd.affine_select(out=ident[:, :], in_=ident[:, :], compare_op=ALU.not_equal, fill=1.0,
                                    base=0, pattern=[[-1, P]], channel_multiplier=1).then_inc(s_const, 1)
            for i in range(LN_GROUPS + 1):
                n, g = group_rows(i)
                b = i % 2
                pool.wait_ge(s_hi, i + 1)
                nc.gpsimd.tensor_tensor(tg[0:n, b, 0:g, D:2 * D], hg[0:n, b, 0:g, :],
                                        tg[0:n, b, 0:g, 0:D], ALU.subtract).then_inc(s_split, 1)
                if i == 1:
                    pool.wait_ge(s_nodes, 32)
                    nc.gpsimd.tensor_tensor(rel[:, :], dst_i[:, :], base_i[:, :], ALU.subtract).then_inc(s_places, 1)
                if i == 2:
                    nc.gpsimd.tensor_tensor(
                        ahead_of.rearrange("p (s k) -> p s k", k=K), base_i[:, :].rearrange("p (s k) -> p s k", k=K),
                        step_node[:, :].unsqueeze(2).broadcast_to([P, STEPS, K]), ALU.subtract).then_inc(s_places, 1)
            for b in range(2):
                pool.wait_ge(s_tab[b], TAB_DONE[b])

            def gather_step(s, count):
                for k in range(count):
                    for g, (a, b) in enumerate(INDEX_GROUPS):
                        if k == a:
                            pool.wait_ge(index_ready, len(INDEX_GROUPS) * s + g + 1)
                    for a, b in BUFFER_GROUPS:
                        if k == a:
                            if not isinstance(s, int) or s > 0:
                                pool.wait_ge(summed, K * (s - 1) + b)
                            pass_gate(pool, pool_passed)
                    nc.gpsimd.indirect_dma_start(
                        out=rows[:, k, :], out_offset=None, in_=table[:, :],
                        in_offset=bass.IndirectOffsetOnAxis(ap=index_now[:, k:k + 1], axis=0),
                    ).then_inc(landed[k], 16)

            pool.wait_ge(s_flag, 1)
            unfit = pool.value_load(unfit_i[0:1, 0:1], min_val=0, max_val=1)
            with pool.If(unfit < 1):
                gather_step(0, K)
                with pool.Fori(1, STEPS - 1) as s:
                    gather_step(s, K)
                gather_step(STEPS - 1, K_LAST)
            with pool.Else():
                pool.wait_ge(g_prep, 1)
                nc.gpsimd.memset(ident32, 0.0).then_inc(s_const, 1)
                nc.gpsimd.memset(before, 1.0).then_inc(s_const, 1)
                nc.gpsimd.iota(spill, [[0, 1]], base=SPILL, channel_multiplier=1,
                               allow_small_or_imprecise_dtypes=True).then_inc(s_const, 1)
                pool.wait_ge(s_const, 5)
                nc.gpsimd.affine_select(out=ident32, in_=ident32, compare_op=ALU.not_equal, fill=1.0,
                                        base=0, pattern=[[-1, P]], channel_multiplier=1).then_inc(s_const, 1)
                nc.gpsimd.affine_select(out=before, in_=before, compare_op=ALU.is_gt, fill=0.0,
                                        base=0, pattern=[[-1, P]], channel_multiplier=1).then_inc(s_const, 1)
                with pool.Fori(0, E_CHUNKS) as c:
                    pool.wait_ge(g_index, c + 1)
                    pass_gate(pool, pool_passed)
                    nc.gpsimd.indirect_dma_start(
                        out=rows[:, 0, :], out_offset=None, in_=table[:, :],
                        in_offset=bass.IndirectOffsetOnAxis(ap=index_now[:, 0:1], axis=0)).then_inc(g_rows, 16)
                    pool.wait_ge(g_target, c + 1)
                    pool.wait_ge(g_copied, c + 1)
                    pass_gate(pool, pool_passed)
                    nc.gpsimd.indirect_dma_start(
                        out=sums_table[:, :], out_offset=bass.IndirectOffsetOnAxis(ap=target, axis=0),
                        in_=chunk_sum, in_offset=None, compute_op=ALU.add).then_inc(g_added, 16)
                pool.wait_ge(g_added, 16 * E_CHUNKS)

        @block.scalar
        def _(act):
            def deviation(i):
                n, g = group_rows(i)
                act.wait_ge(s_var, i + 1)
                if i >= 2:
                    act.wait_ge(s_scale, i - 1)
                nc.scalar.activation(std[0:n, i % 2, 0:g], mv[0:n, i % 2, 0:g, 1], ACT.Sqrt, bias=eps[0:n, :],
                                     scale=HALF ** 2).then_inc(s_std, 1)

            def store_group(i):
                n, g = group_rows(i)
                act.wait_ge(s_split, i + 1)
                act.dma_start(table_group(i), tg[0:n, i % 2, 0:g, :]).then_inc(s_tab[i % 2], 16)

            act.wait_ge(s_eps, 1)
            deviation(0)
            for i in range(LN_GROUPS + 1):
                n, g = group_rows(i)
                b = i % 2
                if i < LN_GROUPS:
                    deviation(i + 1)
                act.wait_ge(s_scale, i + 1)
                act.wait_ge(s_x[i % XB], 16 * (i // XB + 1))
                if i >= 2:
                    act.wait_ge(s_split, i - 1)
                for j in range(GV, g):
                    last = nc.scalar.activation(hg[0:n, b, j, :], xg[0:n, i % XB, j, :], ACT.Relu,
                                                bias=shift[0:n, b, j:j + 1], scale=rstd[0:n, b, j:j + 1])
                if g > GV:
                    last.then_inc(s_norm_act, 1)
                act.wait_ge(s_norm, i + 1)
                v = min(g, GV)
                nc.scalar.activation(hg[0:n, b, 0:v, :], hg[0:n, b, 0:v, :], ACT.Relu).then_inc(s_h, 1)
                act.wait_ge(s_h, i + 1)
                if i >= 2:
                    act.wait_ge(s_tab[b], 16 * (i // 2))
                nc.scalar.copy(tg[0:n, b, 0:g, 0:D], hg[0:n, b, 0:g, :]).then_inc(s_hi, 1)
                if i >= 1:
                    store_group(i - 1)
            store_group(LN_GROUPS)

            def index_group(s, g):
                a, b = INDEX_GROUPS[g]
                nc.scalar.copy(index_now[:, a:b], src_i[:, bass.ds(s * K + a, b - a)]).then_inc(index_ready, 1)

            def stage_tile(t):
                act.wait_ge(carried, t + 1)
                if not isinstance(t, int) or t > 0:
                    act.wait_ge(out_ready, t)
                pass_gate(act, act_passed)
                nc.scalar.copy(stage[:, :, :], ring[:, :, bass.ds(ring_slot(t), P)]).then_inc(staged, 1)
                act.wait_ge(staged, t + 1)
                pass_gate(act, act_passed)
                nc.scalar.copy(ring[:, :, bass.ds(ring_slot(t), SLOT)], zeros[:, :, :]).then_inc(cleared, 1)

            def stage_last(t, to):
                act.wait_ge(carried, t + 1)
                for h in range(H):
                    nc.scalar.copy(to[:, h * R:(h + 1) * R, :],
                                   ring[:, h * R:(h + 1) * R, ring_slot(t):ring_slot(t) + P]).then_inc(last_staged, 1)

            def copy_hT(t, to=own_hT):
                act.wait_ge(hT_ready, t + 1)
                nc.scalar.copy(to[:, :, :], ps_hT[:, 0:D].rearrange("p (h n) -> p h n", h=H)
                               ).then_inc(hT_copied, 1)

            def scalar_step(s, finish, ahead):
                if finish:
                    stage_tile(s - 2)
                for g in range(2):
                    if ahead:
                        act.wait_ge(summed, K * s + INDEX_GROUPS[g][1])
                        pass_gate(act, act_passed)
                        index_group(s + 1, g)
                    if finish and g == 0:
                        copy_hT(s - 2)

            def general_chunk(c):
                general_turn(act, c)
                pass_gate(act, act_passed)
                nc.scalar.copy(index_now[:, 0:1], src_i[:, bass.ds(c, 1)]).then_inc(g_index, 1)
                act.wait_ge(g_sum, c + 1)
                nc.scalar.copy(chunk_sum, ps_out[:, 0:D]).then_inc(g_copied, 1)

            def general_stage(t):
                act.wait_ge(g_turned, t + 1)
                if not isinstance(t, int) or t > 0:
                    act.wait_ge(out_ready, t)
                for q in range(HR // 4):
                    last = nc.scalar.copy(stage[:, 4 * q:4 * q + 4, :],
                                          sums[q][:, :].rearrange("p (a n) -> p a n", a=4))
                last.then_inc(staged, 1)
                copy_hT(t)

            act.wait_ge(s_zeros, 1)
            act.wait_ge(s_src, 16)
            act.wait_ge(s_flag, 1)
            unfit = act.value_load(unfit_i[0:1, 0:1], min_val=0, max_val=1)
            with act.If(unfit < 1):
                for g in range(2):
                    index_group(0, g)
                for s in range(3):
                    scalar_step(s, s >= 2, True)
                with act.Fori(3, STEPS - 1) as s:
                    scalar_step(s, True, True)
                scalar_step(STEPS - 1, True, False)
                act.wait_ge(out_ready, TILES - 2)
                stage_last(TILES - 2, stage)
                copy_hT(TILES - 2)
                stage_last(TILES - 1, last_stage)
                copy_hT(TILES - 1, last_hT)
            with act.Else():
                general_chunk(0)
                with act.Fori(1, E_CHUNKS) as c:
                    general_chunk(c)
                general_stage(0)
                with act.Fori(1, TILES) as t:
                    general_stage(t)

        @block.vector
        def _(dve):
            nc.vector.memset(eps[:, :], EPS * HALF ** 2).then_inc(s_eps, 1)
            steps = [0]

            def link(ins):
                steps[0] += 1
                ins.then_inc(s_prep, 1)
                dve.wait_ge(s_prep, steps[0])

            def statistics(i):
                n, g = group_rows(i)
                b = i % 2
                dve.wait_ge(s_x[i % XB], 16 * (i // XB + 1))
                if i >= 1:
                    dve.wait_ge(s_var, i)
                for j in range(g):
                    last = nc.vector.bn_stats(stats[0:n, j, :], xg[0:n, i % XB, j, :])
                link(last)
                if i >= 2:
                    dve.wait_ge(s_std, i - 1)
                for j in range(g):
                    last = nc.vector.bn_aggr(mv[0:n, b, j, :], stats[0:n, j, :])
                last.then_inc(s_var, 1)

            def normalise(i):
                n, g = group_rows(i)
                b = i % 2
                dve.wait_ge(s_var, i + 1)
                dve.wait_ge(s_std, i + 1)
                if i >= 2:
                    dve.wait_ge(s_hi, i - 1)
                nc.vector.tensor_scalar(mv[0:n, b, 0:g, 1], mv[0:n, b, 0:g, 1], HALF ** 2, EPS * HALF ** 2,
                                        ALU.mult, ALU.add)
                link(nc.vector.reciprocal(root[0:n, 0:g], std[0:n, b, 0:g]))
                link(nc.vector.tensor_tensor(root[0:n, 0:g], root[0:n, 0:g], mv[0:n, b, 0:g, 1], ALU.mult))
                link(nc.vector.tensor_tensor(root[0:n, 0:g], root[0:n, 0:g], std[0:n, b, 0:g], ALU.add))
                link(nc.vector.reciprocal(rstd[0:n, b, 0:g], root[0:n, 0:g]))
                nc.vector.scalar_tensor_tensor(shift[0:n, b, 0:g], mv[0:n, b, 0:g, 0], -1.0, rstd[0:n, b, 0:g],
                                               ALU.mult, ALU.mult).then_inc(s_scale, 1)
                dve.wait_ge(s_scale, i + 1)
                if i >= 2:
                    dve.wait_ge(s_split, i - 1)
                for j in range(min(g, GV)):
                    last = nc.vector.tensor_scalar(hg[0:n, b, j, :], xg[0:n, i % XB, j, :], rstd[0:n, b, j:j + 1],
                                                   shift[0:n, b, j:j + 1], ALU.mult, ALU.add)
                last.then_inc(s_norm, 1)

            def reduced(i, values, op):
                dve.wait_ge(s_places, 2)
                nc.vector.tensor_reduce(unfit_p[:, i:i + 1], values, AX.X, op).then_inc(s_unfit, 1)

            def count_unfit():
                dve.wait_ge(s_unfit, 4)
                nc.vector.tensor_scalar(unfit_p[:, 4:5], unfit_p[:, 0:1], float(W - 1), None, ALU.is_gt)
                nc.vector.tensor_scalar(unfit_p[:, 5:6], unfit_p[:, 1:2], 0.0, None, ALU.is_lt)
                nc.vector.tensor_scalar(unfit_p[:, 6:7], unfit_p[:, 2:3], float(2 * P - W), None, ALU.is_gt)
                nc.vector.tensor_scalar(unfit_p[:, 7:8], unfit_p[:, 3:4], float(-P), None, ALU.is_lt)
                nc.vector.memset(ones[:, :], 1.0).then_inc(s_unfit, 1)

            def judge():
                dve.wait_ge(s_unfit_sum, 1)
                nc.vector.tensor_reduce(unfit_p[0:1, 0:1], ps_out[0:1, 0:4], AX.X, ALU.add).then_inc(s_unfit, 1)
                dve.wait_ge(s_unfit, 6)
                nc.vector.tensor_scalar(unfit_i[:, :], unfit_p[0:1, 0:1], 0.5, None, ALU.is_gt).then_inc(s_flag, 1)

            def edge_slots():
                dve.wait_ge(s_types, 16)
                nc.vector.scalar_tensor_tensor(slot[:, :], type_i[:, :], float(W), rel[:, :],
                                               ALU.mult, ALU.add).then_inc(s_slot, 1)

            def window_tiles():
                nc.vector.tensor_scalar(tile_of, base_i[0:1, :], P.bit_length() - 1, RING - 1,
                                        ALU.arith_shift_right, ALU.bitwise_and).then_inc(s_window, 1)

            def window_rests():
                nc.vector.tensor_scalar(within, base_i[0:1, :], P - 1, None, ALU.bitwise_and).then_inc(s_window, 1)

            def window_offsets():
                dve.wait_ge(s_window, 2)
                nc.vector.scalar_tensor_tensor(
                    offsets[:, :, 0:K], tile_of.rearrange("p (s k) -> p s k", k=K), float(SLOT),
                    within.rearrange("p (s k) -> p s k", k=K), ALU.mult, ALU.add).then_inc(s_window, 1)

            pieces = {
                1: window_tiles, 2: window_rests, 3: window_offsets,
                4: lambda: reduced(0, rel[:, :], ALU.max), 5: lambda: reduced(1, rel[:, :], ALU.min),
                6: lambda: reduced(2, ahead_of, ALU.max), 7: lambda: reduced(3, ahead_of, ALU.min),
                8: count_unfit, 9: judge, 10: edge_slots,
            }
            statistics(0)
            for i in range(LN_GROUPS + 1):
                if i < LN_GROUPS:
                    statistics(i + 1)
                normalise(i)
                if i == 1:
                    dve.wait_ge(s_nodes, 32)
                if i in pieces:
                    pieces[i]()
            dve.wait_ge(s_window, 3)

            def onehot_group(s, g, count=K):
                a, b = ONEHOT_GROUPS[g]
                b = min(b, count)
                if b > a:
                    nc.vector.tensor_tensor(
                        onehot[:, a:b, :], lane[:, :].unsqueeze(1).broadcast_to([P, b - a, P]),
                        slot[:, bass.ds(s * K + a, b - a)].unsqueeze(2).broadcast_to([P, b - a, P]),
                        ALU.is_equal).then_inc(onehot_ready, 1)

            def carry_tile(t):
                head = ring[:, :, bass.ds(ring_slot(t), W)]
                if not isinstance(t, int) or t > 0:
                    dve.wait_ge(carried, t)
                nc.vector.tensor_tensor(head, head, carry[:, :, :], ALU.add).then_inc(spill_added, 1)
                dve.wait_ge(spill_added, t + 1)
                nc.vector.tensor_copy(carry[:, :, :], ring[:, :, bass.ds(ring_slot(t) + P, W)]
                                      ).then_inc(carried, 1)

            def finish_tile(t, n, product=ps_out):
                dve.wait_ge(out_ready, t + 1)
                dve.wait_ge(x_landed, 16 * (t + 1))
                if not isinstance(t, int) or t > 0:
                    dve.wait_ge(stored, 16 * t)
                nc.vector.scalar_tensor_tensor(result[0:n, :], product[0:n, 0:D], C_OUT, own_x[0:n, :],
                                               ALU.mult, ALU.add).then_inc(scaled, 1)
                dve.wait_ge(scaled, t + 1)
                nc.vector.tensor_tensor(result[0:n, :], result[0:n, :], bias_b[0:n, :], ALU.add
                                        ).then_inc(result_ready, 1)

            def vector_step(s, count, closes, finish, ahead, ahead_count=K):
                for k in range(count):
                    if k % 4 == 0:
                        m = min(4, count - k)
                        _, offs = nc.values_load_multi_w_load_instructions(
                            offsets[0:1, bass.ds(s, 1), k:k + m].rearrange("p s k -> p (s k)"),
                            engines=[mybir.EngineType.DVE], min_val=0, max_val=RING * SLOT - W,
                            skip_runtime_bounds_check_because="offset = tile % RING * SLOT + node % P, "
                            "whatever the node, and P - 1 + W < SLOT + 1")
                    if k == 0 and (not isinstance(s, int) or s > 2):
                        dve.wait_ge(cleared, s - 2)
                    dve.wait_ge(summed, K * s + k + 1)
                    if not isinstance(s, int) or s > 0 or k > 0:
                        dve.wait_ge(added, K * s + k)
                    window = ring[:, :, bass.ds(offs[k % 4], W)]
                    nc.vector.tensor_tensor(window, window, sum_of(k).rearrange("p (a w) -> p a w", w=W),
                                            ALU.add).then_inc(added, 1)
                    for g, (a, b) in enumerate(ONEHOT_GROUPS):
                        if ahead and k == b - 1:
                            onehot_group(s + 1, g, ahead_count)
                if closes:
                    carry_tile(s - 1)
                if not ahead:
                    carry_tile(s)
                if finish:
                    finish_tile(s - 2, P)

            def general_chunk(c):
                def done(i):
                    return 6 * c + i

                general_turn(dve, c)
                now = key[:, bass.ds(c, 1)]
                nc.vector.tensor_scalar(diagonal, ident32, now, None, ALU.mult).then_inc(g_diag, 1)
                dve.wait_ge(g_keys, c + 1)
                nc.vector.tensor_scalar(same, ps_hT[:, 0:P], now, None, ALU.is_equal).then_inc(g_same, 1)
                dve.wait_ge(g_same, c + 1)
                nc.vector.tensor_tensor(masked, same, before, ALU.mult).then_inc(g_vec, 1)
                dve.wait_ge(g_vec, done(1))
                nc.vector.tensor_reduce(duplicate, masked, AX.X, ALU.max).then_inc(g_vec, 1)
                dve.wait_ge(g_vec, done(2))
                nc.vector.tensor_scalar(single, duplicate, -1.0, 1.0, ALU.mult, ALU.add).then_inc(g_vec, 1)
                nc.vector.tensor_tensor(moved, now, spill, ALU.subtract).then_inc(g_vec, 1)
                dve.wait_ge(g_vec, done(4))
                nc.vector.tensor_tensor(moved, moved, single, ALU.mult).then_inc(g_vec, 1)
                dve.wait_ge(g_vec, done(5))
                nc.vector.tensor_tensor(target, moved, spill, ALU.add).then_inc(g_vec, 1)
                dve.wait_ge(g_vec, done(6))
                dve.sem_inc(g_target, 1)

            dve.wait_ge(s_flag, 1)
            unfit = dve.value_load(unfit_i[0:1, 0:1], min_val=0, max_val=1)
            with dve.If(unfit < 1):
                dve.wait_ge(s_slot, 1)
                for g in range(len(ONEHOT_GROUPS)):
                    onehot_group(0, g)
                dve.wait_ge(s_zeros, 3)
                for s in range(3):
                    if s == 2:
                        dve.wait_ge(s_w, 16 * (2 * H + 1))
                    vector_step(s, K, s >= 1, s >= 2, True)
                with dve.Fori(3, STEPS - 2) as s:
                    vector_step(s, K, True, True, True)
                vector_step(STEPS - 2, K, True, True, True, K_LAST)
                vector_step(STEPS - 1, K_LAST, True, True, False)
                finish_tile(TILES - 2, P)
                finish_tile(TILES - 1, LAST, last_out)
            with dve.Else():
                dve.wait_ge(s_tab[0], TAB_DONE[0])
                dve.wait_ge(s_tab[1], TAB_DONE[1])
                nc.vector.scalar_tensor_tensor(key[:, :], type_i[:, :], float(PITCH), dst_i[:, :],
                                               ALU.mult, ALU.add).then_inc(g_prep, 1)
                dve.wait_ge(g_prep, 1)
                dve.wait_ge(s_w, 16 * (2 * H + 1))
                dve.wait_ge(s_const, 7)
                general_chunk(0)
                with dve.Fori(1, E_CHUNKS) as c:
                    general_chunk(c)
                finish_tile(0, P)
                with dve.Fori(1, TILES - 1) as t:
                    finish_tile(t, P)
                finish_tile(TILES - 1, LAST)

        @block.tensor
        def _(pe):

            def own_rows(t):
                pe.wait_ge(own_landed, 16 * (t + 1))
                if not isinstance(t, int) or t > 0:
                    pe.wait_ge(hT_copied, t)
                for h in range(H):
                    for part in range(2):
                        last = nc.tensor.matmul(ps_hT[:, h * P:(h + 1) * P],
                                                own[:, part * D + h * P:part * D + (h + 1) * P], ident[:, :],
                                                start=(part == 0), stop=(part == 1))
                last.then_inc(hT_ready, 1)

            def last_product(t, m):
                of, product, hT = ((stage, ps_out, own_hT), (last_stage, last_out, last_hT))[t - (TILES - 2)]
                if m in (0, R):
                    pe.wait_ge(last_staged, H * (t - (TILES - 2)) + m // R + 1)
                if m == 0 and t == TILES - 2:
                    pe.wait_ge(result_ready, t)
                if m == HR:
                    pe.wait_ge(hT_copied, t + 1)
                h, r = (m // R, m % R) if m < HR else (m - HR, R)
                lhs = of[:, m, :] if m < HR else hT[:, h, :]
                last = nc.tensor.matmul(product[:, 0:D], lhs, w_sb[:, h, r, :], start=(m == 0), stop=(m == HR + H - 1))
                if m == HR + H - 1:
                    last.then_inc(out_ready, 1)

            def tile_product(t, m):
                if m == 0:
                    pe.wait_ge(staged, t + 1)
                    if not isinstance(t, int) or t > 0:
                        pe.wait_ge(result_ready, t)
                if m < HR:
                    h, r = m // R, m % R
                    nc.tensor.matmul(ps_out[:, 0:D], stage[:, m, :], w_sb[:, h, r, :], start=(m == 0), stop=False)
                else:
                    h = m - HR
                    if h == 0:
                        pe.wait_ge(hT_copied, t + 1)
                    last = nc.tensor.matmul(ps_out[:, 0:D], own_hT[:, h, :], w_sb[:, h, R, :],
                                            start=False, stop=(h == H - 1))
                    if h == H - 1:
                        last.then_inc(out_ready, 1)

            def tensor_step(s, count, finish, begin=8):
                products = list(range(HR + H)) if finish else []
                for k in range(count):
                    for g, (a, b) in enumerate(ONEHOT_GROUPS):
                        if k == a:
                            pe.wait_ge(onehot_ready, len(ONEHOT_GROUPS) * s + g + 1)
                    if not isinstance(s, int) or s > 0:
                        pe.wait_ge(landed[k], 16 * (s + 1))
                        pe.wait_ge(added, K * s + k - NSUM + 1 if k >= NSUM
                                   else K * (s - 1) + K - (K - 1 - k) % NSUM)
                    else:
                        pe.wait_ge(landed[k], 16)
                        if k >= NSUM:
                            pe.wait_ge(added, k - NSUM + 1)
                    for h in range(H):
                        for part in range(2):
                            last = nc.tensor.matmul(sum_of(k)[:, h * P:(h + 1) * P],
                                                    rows[:, k, part * D + h * P:part * D + (h + 1) * P],
                                                    onehot[:, k, :], start=(part == 0), stop=(part == 1))
                    last.then_inc(summed, 1)
                    if finish and k == 3:
                        own_rows(s - 2)
                    if k >= begin:
                        now = 2 if len(products) > count - 2 - k else 1
                        for m in products[:now]:
                            tile_product(s - 2, m)
                        products = products[now:]
                for m in products:
                    tile_product(s - 2, m)

            def whole_tile(t):
                own_rows(t)
                for m in range(HR + H):
                    tile_product(t, m)

            def general_chunk(c):
                pe.wait_ge(g_diag, c + 1)
                nc.tensor.matmul(ps_hT[:, 0:P], ones[:, :], diagonal, start=True, stop=True).then_inc(g_keys, 1)
                pe.wait_ge(g_same, c + 1)
                pe.wait_ge(g_rows, 16 * (c + 1))
                nc.tensor.matmul(ps_out[:, 0:D], same, rows[:, 0, 0:D], start=True, stop=False)
                nc.tensor.matmul(ps_out[:, 0:D], same, rows[:, 0, D:2 * D], start=False, stop=True
                                 ).then_inc(g_sum, 1)

            def general_tile(t):
                pe.wait_ge(g_tile, 16 * (t + 1))
                if not isinstance(t, int) or t > 0:
                    pe.wait_ge(staged, t)
                for m in range(HR):
                    h, r = m // R, m % R
                    last = nc.tensor.matmul(sums[m // 4][:, m % 4 * P:(m % 4 + 1) * P],
                                            tile_sums[:, r, h * P:(h + 1) * P], ident32, start=True, stop=True)
                last.then_inc(g_turned, 1)
                whole_tile(t)

            pe.wait_ge(s_unfit, 5)
            nc.tensor.matmul(ps_out[0:1, 0:4], ones[:, 0:1], unfit_p[:, 4:8], start=True, stop=True
                             ).then_inc(s_unfit_sum, 1)
            pe.wait_ge(s_const, 2)
            pe.wait_ge(s_flag, 1)
            unfit = pe.value_load(unfit_i[0:1, 0:1], min_val=0, max_val=1)
            with pe.If(unfit < 1):
                for s in range(3):
                    if s == 2:
                        pe.wait_ge(s_w, 16 * (2 * H + 1))
                    tensor_step(s, K, s >= 2)
                with pe.Fori(3, STEPS - 1) as s:
                    tensor_step(s, K, True)
                tensor_step(STEPS - 1, K_LAST, True, 5)
                own_rows(TILES - 2)
                for m in range(HR + H):
                    last_product(TILES - 2, m)
                    if m == HR // 2:
                        own_rows(TILES - 1)
                for m in range(HR + H):
                    last_product(TILES - 1, m)
            with pe.Else():
                pe.wait_ge(s_w, 16 * (2 * H + 1))
                pe.wait_ge(s_const, 7)
                with pe.Fori(0, E_CHUNKS) as c:
                    general_chunk(c)
                pe.wait_ge(g_copied, E_CHUNKS)
                general_tile(0)
                with pe.Fori(1, TILES) as t:
                    general_tile(t)


def kernel(x, src, dst, edge_type_8, L0_gnn_weight, L0_gnn_h_bias, L0_gnn_loop_weight):
    import numpy as np
    import concourse.bacc as bacc
    from concourse.bass_utils import run_bass_kernel_spmd as run

    P = 128
    n, d = x.shape
    edges = src.shape[0]
    tiles = -(-n // P)
    chunks = -(-edges // P)
    padded = -(-chunks // tiles) * tiles

    def by_chunk(a, fill):
        flat = np.full(padded * P, fill, np.int32)
        flat[:edges] = np.asarray(a)
        return np.ascontiguousarray(flat.reshape(padded, P).T)

    arrays = {
        "x": np.ascontiguousarray(x),
        "src": by_chunk(src, 0),
        "dst": by_chunk(dst, n),
        "etype": by_chunk(edge_type_8, 0),
        "weight": np.ascontiguousarray(L0_gnn_weight),
        "h_bias": np.ascontiguousarray(L0_gnn_h_bias).reshape(1, d),
        "loop_weight": np.ascontiguousarray(L0_gnn_loop_weight),
    }
    nc = bacc.Bacc("TRN2", target_bir_lowering=False, num_devices=1)
    args = [nc.dram_tensor(k, a.shape, mybir.dt.from_np(a.dtype), kind="ExternalInput").ap() for k, a in arrays.items()]
    out = nc.dram_tensor("out", (n, d), mybir.dt.float32, kind="ExternalOutput").ap()
    relational_graph_layer(nc, *args, out, chunks)
    return run(nc, [arrays], core_ids=[0]).results[0]["out"]
```
